# Optimizing a Trainium2 kernel written in Bass

```python
import numpy as np
import jax
import jax.numpy as jnp

def _softmax(x, axis=-1):
    return jax.nn.softmax(x, axis=axis)

def _gelu(x):
    return jax.nn.gelu(x, approximate=True)

def _silu(x):
    return jax.nn.silu(x)

def _sigmoid(x):
    return jax.nn.sigmoid(x)

def _layernorm(x, axis=-1, eps=1e-05):
    m = jnp.mean(x, axis=axis, keepdims=True)
    v = jnp.var(x, axis=axis, keepdims=True)
    return (x - m) / jnp.sqrt(v + eps)

def _scatter_add(tgt, idx, src, axis=0):
    return tgt.at[idx].add(src)

def _segment_sum(src, seg, n):
    return jax.ops.segment_sum(src, seg, n)
kernel_name = 'mk_dlrm_tower_d1_rec_r8_ae0b7b'

def setup_inputs(seed: int=0):
    np.random.seed(seed)
    _w = jnp.asarray

    def _rec_inputs():
        import jax
        import jax.numpy as jnp
        _tk = jax.random.key(seed)
        dense_ctx = jax.random.normal(jax.random.fold_in(_tk, 190), (2048, 16), jnp.float32)
        ids = jnp.stack([jax.random.randint(jax.random.fold_in(_tk, 200 + f), (2048,), 0, v, jnp.int32) for f, v in enumerate([1250, 1000, 1250, 1250, 1000, 125000, 1000, 1250, 1000, 1250, 1250, 1250, 1000, 1250, 1250, 12500, 12500, 1000, 1250, 1250, 1250, 1250, 1250, 12500, 12500, 12500, 1250])], axis=1)
        tbl_0 = 0.05 * jax.random.normal(jax.random.fold_in(_tk, 500 + 0), (1250, 128), jnp.float32)
        tbl_1 = 0.05 * jax.random.normal(jax.random.fold_in(_tk, 500 + 1), (1000, 128), jnp.float32)
        tbl_2 = 0.05 * jax.random.normal(jax.random.fold_in(_tk, 500 + 2), (1250, 128), jnp.float32)
        tbl_3 = 0.05 * jax.random.normal(jax.random.fold_in(_tk, 500 + 3), (1250, 128), jnp.float32)
        tbl_4 = 0.05 * jax.random.normal(jax.random.fold_in(_tk, 500 + 4), (1000, 128), jnp.float32)
        tbl_5 = 0.05 * jax.random.normal(jax.random.fold_in(_tk, 500 + 5), (125000, 128), jnp.float32)
        tbl_6 = 0.05 * jax.random.normal(jax.random.fold_in(_tk, 500 + 6), (1000, 128), jnp.float32)
        tbl_7 = 0.05 * jax.random.normal(jax.random.fold_in(_tk, 500 + 7), (1250, 128), jnp.float32)
        tbl_8 = 0.05 * jax.random.normal(jax.random.fold_in(_tk, 500 + 8), (1000, 128), jnp.float32)
        tbl_9 = 0.05 * jax.random.normal(jax.random.fold_in(_tk, 500 + 9), (1250, 128), jnp.float32)
        tbl_10 = 0.05 * jax.random.normal(jax.random.fold_in(_tk, 500 + 10), (1250, 128), jnp.float32)
        tbl_11 = 0.05 * jax.random.normal(jax.random.fold_in(_tk, 500 + 11), (1250, 128), jnp.float32)
        tbl_12 = 0.05 * jax.random.normal(jax.random.fold_in(_tk, 500 + 12), (1000, 128), jnp.float32)
        tbl_13 = 0.05 * jax.random.normal(jax.random.fold_in(_tk, 500 + 13), (1250, 128), jnp.float32)
        tbl_14 = 0.05 * jax.random.normal(jax.random.fold_in(_tk, 500 + 14), (1250, 128), jnp.float32)
        tbl_15 = 0.05 * jax.random.normal(jax.random.fold_in(_tk, 500 + 15), (12500, 128), jnp.float32)
        tbl_16 = 0.05 * jax.random.normal(jax.random.fold_in(_tk, 500 + 16), (12500, 128), jnp.float32)
        tbl_17 = 0.05 * jax.random.normal(jax.random.fold_in(_tk, 500 + 17), (1000, 128), jnp.float32)
        tbl_18 = 0.05 * jax.random.normal(jax.random.fold_in(_tk, 500 + 18), (1250, 128), jnp.float32)
        tbl_19 = 0.05 * jax.random.normal(jax.random.fold_in(_tk, 500 + 19), (1250, 128), jnp.float32)
        tbl_20 = 0.05 * jax.random.normal(jax.random.fold_in(_tk, 500 + 20), (1250, 128), jnp.float32)
        tbl_21 = 0.05 * jax.random.normal(jax.random.fold_in(_tk, 500 + 21), (1250, 128), jnp.float32)
        tbl_22 = 0.05 * jax.random.normal(jax.random.fold_in(_tk, 500 + 22), (1250, 128), jnp.float32)
        tbl_23 = 0.05 * jax.random.normal(jax.random.fold_in(_tk, 500 + 23), (12500, 128), jnp.float32)
        tbl_24 = 0.05 * jax.random.normal(jax.random.fold_in(_tk, 500 + 24), (12500, 128), jnp.float32)
        tbl_25 = 0.05 * jax.random.normal(jax.random.fold_in(_tk, 500 + 25), (12500, 128), jnp.float32)
        tbl_26 = 0.05 * jax.random.normal(jax.random.fold_in(_tk, 500 + 26), (1250, 128), jnp.float32)
        _rk = jax.random.fold_in(_tk, 7)
        W_top1 = 0.0521996 * jax.random.normal(jax.random.fold_in(_tk, 801), (367, 512), jnp.float32)
        W_top2 = 0.0441942 * jax.random.normal(jax.random.fold_in(_tk, 802), (512, 256), jnp.float32)
        W_top3 = 0.0625 * jax.random.normal(jax.random.fold_in(_tk, 803), (256, 1), jnp.float32)
        b_top1 = jnp.zeros((512,), jnp.float32)
        b_top2 = jnp.zeros((256,), jnp.float32)
        return (dense_ctx, ids, tbl_0, tbl_1, tbl_2, tbl_3, tbl_4, tbl_5, tbl_6, tbl_7, tbl_8, tbl_9, tbl_10, tbl_11, tbl_12, tbl_13, tbl_14, tbl_15, tbl_16, tbl_17, tbl_18, tbl_19, tbl_20, tbl_21, tbl_22, tbl_23, tbl_24, tbl_25, tbl_26, W_top1, b_top1, W_top2, b_top2, W_top3)
    dense_ctx, ids, tbl_0, tbl_1, tbl_2, tbl_3, tbl_4, tbl_5, tbl_6, tbl_7, tbl_8, tbl_9, tbl_10, tbl_11, tbl_12, tbl_13, tbl_14, tbl_15, tbl_16, tbl_17, tbl_18, tbl_19, tbl_20, tbl_21, tbl_22, tbl_23, tbl_24, tbl_25, tbl_26, W_top1, b_top1, W_top2, b_top2, W_top3 = _rec_inputs()

    def _L0_rec_setup():
        import jax, jax.numpy as jnp
        import numpy as np
        NUM_FEATURES = 27
        EMBED_DIM = 128
        BATCH = 4096
        key = jax.random.key(seed)
        inputs = jax.random.normal(key, (BATCH, NUM_FEATURES, EMBED_DIM), dtype=jnp.float32)
        return {'inputs': inputs}
    _L0_rec_all = _L0_rec_setup()
    _L0_rec_in = {k: v for k, v in _L0_rec_all.items() if k in ()}
    del _L0_rec_all
    return {'dense_ctx': dense_ctx, 'ids': ids, 'tbl_0': tbl_0, 'tbl_1': tbl_1, 'tbl_2': tbl_2, 'tbl_3': tbl_3, 'tbl_4': tbl_4, 'tbl_5': tbl_5, 'tbl_6': tbl_6, 'tbl_7': tbl_7, 'tbl_8': tbl_8, 'tbl_9': tbl_9, 'tbl_10': tbl_10, 'tbl_11': tbl_11, 'tbl_12': tbl_12, 'tbl_13': tbl_13, 'tbl_14': tbl_14, 'tbl_15': tbl_15, 'tbl_16': tbl_16, 'tbl_17': tbl_17, 'tbl_18': tbl_18, 'tbl_19': tbl_19, 'tbl_20': tbl_20, 'tbl_21': tbl_21, 'tbl_22': tbl_22, 'tbl_23': tbl_23, 'tbl_24': tbl_24, 'tbl_25': tbl_25, 'tbl_26': tbl_26, 'W_top1': W_top1, 'b_top1': b_top1, 'W_top2': W_top2, 'b_top2': b_top2, 'W_top3': W_top3}

def reference(dense_ctx, ids, tbl_0, tbl_1, tbl_2, tbl_3, tbl_4, tbl_5, tbl_6, tbl_7, tbl_8, tbl_9, tbl_10, tbl_11, tbl_12, tbl_13, tbl_14, tbl_15, tbl_16, tbl_17, tbl_18, tbl_19, tbl_20, tbl_21, tbl_22, tbl_23, tbl_24, tbl_25, tbl_26, W_top1, b_top1, W_top2, b_top2, W_top3):
    import jax
    import jax.numpy as jnp

    def _L0_rec_ref(inputs):
        import jax, jax.numpy as jnp
        import numpy as np
        NUM_FEATURES = 27
        EMBED_DIM = 128
        BATCH = 4096
        interactions = jnp.einsum('bnd,bmd->bnm', inputs, inputs)
        n = inputs.shape[1]
        i, j = jnp.triu_indices(n, k=1)
        return interactions[:, i, j]
    e = jnp.stack([tbl_0[ids[:, 0]], tbl_1[ids[:, 1]], tbl_2[ids[:, 2]], tbl_3[ids[:, 3]], tbl_4[ids[:, 4]], tbl_5[ids[:, 5]], tbl_6[ids[:, 6]], tbl_7[ids[:, 7]], tbl_8[ids[:, 8]], tbl_9[ids[:, 9]], tbl_10[ids[:, 10]], tbl_11[ids[:, 11]], tbl_12[ids[:, 12]], tbl_13[ids[:, 13]], tbl_14[ids[:, 14]], tbl_15[ids[:, 15]], tbl_16[ids[:, 16]], tbl_17[ids[:, 17]], tbl_18[ids[:, 18]], tbl_19[ids[:, 19]], tbl_20[ids[:, 20]], tbl_21[ids[:, 21]], tbl_22[ids[:, 22]], tbl_23[ids[:, 23]], tbl_24[ids[:, 24]], tbl_25[ids[:, 25]], tbl_26[ids[:, 26]]], axis=1)
    z = _L0_rec_ref(e)
    z = z.reshape(z.shape[0], -1)
    h = jnp.concatenate([z, dense_ctx], axis=1)
    h = jnp.maximum(h @ W_top1 + b_top1, 0.0)
    h = jnp.maximum(h @ W_top2 + b_top2, 0.0)
    y = h @ W_top3
    return y

_drawn_inputs = setup_inputs


def setup_inputs(seed=0):
    import zlib

    import numpy as np

    out = dict(_drawn_inputs(seed))
    spreads = {'b_top1': (0.0, 0.1), 'b_top2': (0.0, 0.1)}
    factors = {}
    for name, (base, spread) in spreads.items():
        noise = np.random.default_rng([zlib.crc32(name.encode()), seed]).standard_normal(out[name].shape)
        drawn = base * np.exp(spread * noise) if base else spread * noise
        out[name] = jnp.asarray(drawn.astype(out[name].dtype))
    for name, factor in factors.items():
        out[name] = (out[name] * factor).astype(out[name].dtype)
    return out
```

```python
import numpy as np
import concourse.bass as bass
from concourse import mybir
from contextlib import ExitStack

P = 128
BATCH, NF, D, ND = 2048, 27, 128, 16
ROWS = [1250, 1000, 1250, 1250, 1000, 125000, 1000, 1250, 1000, 1250, 1250, 1250, 1000, 1250, 1250,
        12500, 12500, 1000, 1250, 1250, 1250, 1250, 1250, 12500, 12500, 12500, 1250]
H1, H2 = 512, 256

NOH = 7
ONEHOT = sorted(range(NF), key=lambda f: ROWS[f])[:NOH]
GATHER = [f for f in range(NF) if f not in ONEHOT]
ORDER = GATHER + ONEHOT
NG = len(GATHER)
KR = 125
KT = [ROWS[f] // KR for f in ONEHOT]
PARTS = 3

PAIR = 2 * P
NPAIR = BATCH // PAIR
FG = 4
TG = NG // FG
FP = 32
GS = P // 4
GB = 4
NGB = GS // GB
HALF = (NF - 1) // 2
NZ = NF * HALF
ZROW = NF + HALF
NIN = NZ + ND
KC = -(-NIN // P)
LAST = NIN - (KC - 1) * P


def first_layer_rows():
    i, j = np.triu_indices(NF, k=1)
    number = {(int(a), int(b)): n for n, (a, b) in enumerate(zip(i, j))}
    rows = []
    for a in range(NF):
        for k in range(1, HALF + 1):
            x, y = ORDER[a], ORDER[(a + k) % NF]
            rows.append(number[min(x, y), max(x, y)])
    return rows + list(range(NZ, NIN))


def wait(eng, sem, value):
    if not isinstance(value, int) or value > 0:
        eng.wait_ge(sem, value)


def dlrm_tower(nc, ids, ids_t, dense, tables, w1, b1, w2, b2, w3, out):
    fp32, bf16, fp16, i32 = mybir.dt.float32, mybir.dt.bfloat16, mybir.dt.float16, mybir.dt.int32
    ALU, ACT = mybir.AluOpType, mybir.ActivationFunctionType
    ctx = ExitStack()
    with ctx:
        def sb(name, shape, dt):
            return ctx.enter_context(nc.sbuf_tensor(name, shape, dt))

        def sem(name):
            return ctx.enter_context(nc.semaphore(name))

        rows = [sb(f"rows{s}", [P, NG, D], fp32) for s in range(2)]
        emb = sb("emb", [P, 2 * P * FP], fp32)
        emb_g = emb[:, :].rearrange("p (s g q f) -> p s g q f", s=2, g=GS, q=4)
        emb_w = emb[:, :].rearrange("p (s g q f) -> p s f q g", s=2, g=GS, q=4)
        raw = [sb(f"raw{s}", [KR, max(KT), D], fp32) for s in range(2)]
        tab = [sb(f"tab{f}", [KR, PARTS, KT[f], D], bf16) for f in range(NOH)]
        onehot = [sb(f"onehot{f}", [KR, KT[f], PAIR], bf16) for f in range(NOH)]
        idx = [sb(f"idx{s}", [P, NF], i32) for s in range(2)]
        idb = sb("idb", [KR, NOH, PAIR], i32)
        idh = sb("idh", [KR, NOH, PAIR], fp16)
        rown_i = sb("rown_i", [KR, sum(sorted(set(KT)))], i32)
        rown = sb("rown", [KR, sum(sorted(set(KT)))], fp32)
        ident = sb("ident", [P, P], fp32)
        gram = [sb(f"gram{s}", [P, GS, NF], fp32) for s in range(2)]
        zrow = sb("zrow", [P, NF, ZROW], fp32)
        zin = [sb(f"zin{s}", [P, KC * P], fp32) for s in range(2)]
        h0 = sb("h0", [P, KC, PAIR], fp32)
        h1 = sb("h1", [P, H1 // P, PAIR], fp32)
        h2 = sb("h2", [P, H2 // P, PAIR], fp32)
        ysb = sb("ysb", [1, BATCH], fp32)
        w1s = sb("w1s", [P, KC, H1], fp32)
        w2s = sb("w2s", [P, H1 // P, H2], fp32)
        w3s = sb("w3s", [P, H2 // P], fp32)
        b1s = sb("b1s", [P, H1 // P], fp32)
        b2s = sb("b2s", [P, H2 // P], fp32)

        def bank(name):
            return ctx.enter_context(nc.psum_tensor(name, [P, 512], fp32))

        tb = [bank(f"tb{i}") for i in range(2)]
        gb = [bank(f"gb{i}") for i in range(2)]
        xb = [bank(f"xb{i}") for i in range(2)]
        mb = [bank(f"mb{i}") for i in range(2)]

        s_ident = sem("identity_built")
        s_rowi = sem("row_numbers_built")
        s_rown = sem("row_numbers_cast")
        s_zero = sem("pads_zeroed")
        s_idx = [sem(f"ids_loaded{s}") for s in range(2)]
        s_idb = sem("onehot_ids_loaded")
        s_idh = sem("onehot_ids_cast")
        s_free = sem("rows_free")
        s_oh = sem("onehot_made")
        s_raw = [sem(f"table_loaded{s}") for s in range(2)]
        s_hi = sem("table_high")
        s_rest = sem("table_rest")
        s_mid = sem("table_mid")
        s_tab = sem("table_split")
        s_wts = sem("weights_loaded")
        s_rows = [[sem(f"gathered{s}_{g}") for g in range(TG)] for s in range(2)]
        s_t, s_tf = sem("transposed"), sem("transposed_copied")
        s_g = sem("gram_done")
        s_gf = [sem(f"gram_copied{i}") for i in range(2)]
        s_x = [sem(f"x_done{i}") for i in range(2)]
        s_xf = [sem(f"x_copied{i}") for i in range(2)]
        s_m, s_mf = sem("layer_done"), sem("layer_copied")
        s_zt, s_zd, s_z = sem("products_turned"), sem("products_repeated"), sem("inputs_packed")
        s_dense = [sem(f"dense_loaded{s}") for s in range(2)]
        s_out = sem("out_stored")

        def x1_inputs(p, s):
            return p * 5 + 4 + s

        def x_onehot(p, f):
            return p * 4 + f // 2 + 1 if f % 2 == 0 else p * 5 + (f + 1) // 2

        tcol = {t: sum(x for x in sorted(set(KT)) if x < t) for t in set(KT)}
        block = ctx.enter_context(nc.Block())

        @block.sync
        def _(sp):
            def load_ids(p, s):
                sp.dma_start(idx[s][:, :], ids[bass.ds((p * 2 + s) * P, P), :]).then_inc(s_idx[s], 16)

            def load_onehot_ids(p):
                src = ids_t[:, bass.ds(p * PAIR, PAIR)].rearrange("(o f) b -> o f b", o=1).to_broadcast([KR, NOH, PAIR])
                sp.dma_start(idb[:, :, :], src).then_inc(s_idb, 16)

            def load_dense(p, s):
                wait(sp, s_x[1], x1_inputs(p - 1, s))
                sp.dma_start(zin[s][:, NZ:NIN], dense[bass.ds((p * 2 + s) * P, P), :]).then_inc(s_dense[s], 16)

            def step(p, last):
                load_dense(p, 0)
                load_dense(p, 1)
                if not last:
                    for g in range(TG):
                        sp.wait_ge(s_rows[0][g], p * 64 + 64)
                    load_ids(p + 1, 0)
                    sp.wait_ge(s_idh, p + 1)
                    load_onehot_ids(p + 1)
                if not last:
                    for g in range(TG):
                        sp.wait_ge(s_rows[1][g], p * 64 + 64)
                    load_ids(p + 1, 1)

            load_ids(0, 0)
            load_ids(0, 1)
            load_onehot_ids(0)
            for f in range(NOH):
                if f >= 2:
                    sp.wait_ge(s_tab, f - 1)
                src = tables[ONEHOT[f]].rearrange("(p t) d -> p t d", t=KT[f])
                sp.dma_start(raw[f % 2][:, 0:KT[f], :], src).then_inc(s_raw[f % 2], 16)
            sp.dma_start(w1s[:, 0:KC - 1, :], w1[0:(KC - 1) * P, :].rearrange("(c p) n -> p c n", p=P)).then_inc(s_wts, 16)
            sp.dma_start(w1s[0:LAST, KC - 1, :], w1[(KC - 1) * P:NIN, :]).then_inc(s_wts, 16)
            sp.dma_start(w2s[:, :, :], w2.rearrange("(c p) n -> p c n", p=P)).then_inc(s_wts, 16)
            sp.dma_start(w3s[:, :], w3).then_inc(s_wts, 16)
            sp.dma_start(b1s[:, :], b1).then_inc(s_wts, 16)
            sp.dma_start(b2s[:, :], b2).then_inc(s_wts, 16)
            step(0, False)
            with sp.Fori(1, NPAIR - 1) as p:
                step(p, False)
            step(NPAIR - 1, True)
            sp.wait_ge(s_mf, 4 * NPAIR)
            sp.dma_start(out.rearrange("b o -> o b"), ysb[:, :]).then_inc(s_out, 16)
            sp.wait_ge(s_out, 16)

        @block.gpsimd
        def _(pool):
            def gather(p, s):
                pool.wait_ge(s_idx[s], p * 16 + 16)
                for g in range(TG):
                    wait(pool, s_t, (p - 1) * 2 * TG + s * TG + g + 1)
                    pool.sem_inc(s_free, 1)
                    for j in range(FG * g, FG * g + FG):
                        f = GATHER[j]
                        pool.indirect_dma_start(
                            out=rows[s][:, j, :], out_offset=None, in_=tables[f][:, :],
                            in_offset=bass.IndirectOffsetOnAxis(ap=idx[s][:, f:f + 1], axis=0),
                        ).then_inc(s_rows[s][g], 16)

            for t in sorted(set(KT)):
                pool.iota(rown_i[:, tcol[t]:tcol[t] + t], pattern=[[1, t]], base=0, channel_multiplier=t).then_inc(s_rowi, 1)
            pool.memset(ident[:, :], 0.0).then_inc(s_ident, 1)
            pool.wait_ge(s_ident, 1)
            pool.affine_select(out=ident[:, :], in_=ident[:, :], compare_op=ALU.not_equal, fill=1.0, base=0,
                               pattern=[[-1, P]], channel_multiplier=1).then_inc(s_ident, 1)
            for s in range(2):
                gather(0, s)
            with pool.Fori(1, NPAIR) as p:
                for s in range(2):
                    gather(p, s)

        @block.vector
        def _(dve):
            def make_onehot(p, f):
                if f == 0:
                    dve.wait_ge(s_idh, p + 1)
                wait(dve, s_x[f % 2], x_onehot(p - 1, f))
                for t in range(KT[f]):
                    ins = dve.tensor_scalar(onehot[f][:, t, :], idh[:, f, :],
                                            rown[:, tcol[KT[f]] + t:tcol[KT[f]] + t + 1], None, ALU.is_equal)
                ins.then_inc(s_oh, 1)

            def copy_gram(p, s, k):
                dve.wait_ge(s_g, p * 16 + s * NGB + k + 1)
                if k == 1:
                    wait(dve, s_zt, (p - 1) * 2 + s + 1)
                for q in range(4):
                    ins = dve.tensor_copy(
                        gram[s][32 * q:32 * q + 32, GB * k:GB * k + GB, :],
                        gb[1][32 * q:32 * q + 32, 0:GB * 4 * NF].rearrange("p (g c) -> p g c", g=GB)[:, :, NF * q:NF * q + NF])
                ins.then_inc(s_gf[1], 1)

            def pack_inputs(p, s):
                n = p * 2 + s
                dve.wait_ge(s_gf[0], p * 8 + 4 * s + 4)
                dve.wait_ge(s_gf[1], p * 8 + 4 * s + 4)
                wait(dve, s_z, n)
                dve.transpose(zrow[:, :, 0:FP], gram[s][:, :, :].rearrange("p g f -> p f g")).then_inc(s_zt, 1)
                dve.wait_ge(s_zt, n + 1)
                dve.tensor_copy(zrow[:, HALF + 1:NF, NF:ZROW], zrow[:, HALF + 1:NF, 0:HALF]).then_inc(s_zd, 1)
                dve.wait_ge(s_zd, n + 1)
                wait(dve, s_x[1], x1_inputs(p - 1, s))
                flat = zrow[:, :, :].rearrange("p a c -> p (a c)")
                diagonal = bass.AP(tensor=flat.tensor, offset=flat.offset + 1,
                                   ap=[list(flat.ap[0]), [ZROW + 1, NF], [1, HALF]])
                dve.tensor_copy(zin[s][:, 0:NZ].rearrange("p (a k) -> p a k", a=NF), diagonal).then_inc(s_z, 1)

            def step(p, last):
                if not last:
                    for f in range(NOH):
                        make_onehot(p + 1, f)
                for s in range(2):
                    for k in range(1, NGB, 2):
                        copy_gram(p, s, k)
                    pack_inputs(p, s)

            for s in range(2):
                dve.memset(zin[s][:, NIN:KC * P], 0.0)
            dve.memset(emb[:, :].rearrange("p (b f) -> p b f", f=FP)[:, :, NF:FP], 0.0).then_inc(s_zero, 1)
            dve.wait_ge(s_rowi, len(set(KT)))
            dve.tensor_copy(rown[:, :], rown_i[:, :]).then_inc(s_rown, 1)
            dve.wait_ge(s_rown, 1)
            for f in range(NOH):
                make_onehot(0, f)
                w = raw[f % 2][:, 0:KT[f], :]
                dve.wait_ge(s_hi, f + 1)
                dve.tensor_tensor(w, w, tab[f][:, 0, :, :], ALU.subtract).then_inc(s_rest, 1)
                dve.wait_ge(s_mid, f + 1)
                dve.tensor_tensor(tab[f][:, 2, :, :], w, tab[f][:, 1, :, :], ALU.subtract).then_inc(s_tab, 1)
            step(0, False)
            with dve.Fori(1, NPAIR - 1) as p:
                step(p, False)
            step(NPAIR - 1, True)

        @block.scalar
        def _(act):
            def cast_ids(p):
                act.wait_ge(s_idb, p * 16 + 16)
                wait(act, s_oh, p * NOH)
                act.activation(idh[:, :, :], idb[:, :, :], ACT.Copy).then_inc(s_idh, 1)

            def copy_onehot(p, f):
                act.wait_ge(s_x[f % 2], x_onehot(p, f))
                if f == 0:
                    wait(act, s_g, p * 16)
                act.activation(emb_w[:, :, NG + f, :, :], xb[f % 2][:, 0:PAIR].rearrange("p (s q g) -> p s q g", s=2, q=4),
                               ACT.Copy).then_inc(s_xf[f % 2], 1)

            def copy_transposed(p, s, g):
                act.wait_ge(s_t, p * 2 * TG + s * TG + g + 1)
                act.activation(emb_w[:, s, FG * g:FG * g + FG, :, :],
                               tb[(s * TG + g) % 2][:, :].rearrange("p (f q b) -> p f q b", f=FG, q=4), ACT.Copy).then_inc(s_tf, 1)

            def copy_gram(p, s, k):
                act.wait_ge(s_g, p * 16 + s * NGB + k + 1)
                if k == 0:
                    wait(act, s_zt, (p - 1) * 2 + s + 1)
                for q in range(4):
                    ins = act.activation(
                        gram[s][32 * q:32 * q + 32, GB * k:GB * k + GB, :],
                        gb[0][32 * q:32 * q + 32, 0:GB * 4 * NF].rearrange("p (g c) -> p g c", g=GB)[:, :, NF * q:NF * q + NF],
                        ACT.Copy)
                ins.then_inc(s_gf[0], 1)

            def copy_inputs(p, s):
                act.wait_ge(s_x[1], x1_inputs(p, s))
                if s == 0:
                    wait(act, s_m, p * 4 - 2)
                act.activation(h0[:, :, s * P:s * P + P], xb[1][:, 0:KC * P].rearrange("p (c b) -> p c b", c=KC),
                               ACT.Copy).then_inc(s_xf[1], 1)

            def copy_layer(p, u):
                act.wait_ge(s_m, p * 4 + u + 1)
                if u < 2:
                    for c in range(2):
                        ins = act.activation(h1[:, 2 * u + c, :], mb[u][:, c * PAIR:c * PAIR + PAIR], ACT.Relu,
                                             bias=b1s[:, 2 * u + c:2 * u + c + 1])
                elif u == 2:
                    for c in range(2):
                        ins = act.activation(h2[:, c, :], mb[0][:, c * PAIR:c * PAIR + PAIR], ACT.Relu, bias=b2s[:, c:c + 1])
                else:
                    ins = act.activation(ysb[:, bass.ds(p * PAIR, PAIR)], mb[1][0:1, 0:PAIR], ACT.Copy)
                ins.then_inc(s_mf, 1)

            def step(p, first, last):
                if not last:
                    cast_ids(p + 1)
                copy_onehot(p, 0)
                if not first:
                    copy_inputs(p - 1, 1)
                copy_onehot(p, 1)
                if not first:
                    copy_layer(p - 1, 0)
                    copy_layer(p - 1, 1)
                copy_onehot(p, 2)
                if not first:
                    copy_layer(p - 1, 2)
                copy_onehot(p, 3)
                if not first:
                    copy_layer(p - 1, 3)
                for g in range(TG):
                    copy_transposed(p, 0, g)
                    if 4 + g < NOH:
                        copy_onehot(p, 4 + g)
                for k in range(0, NGB, 2):
                    copy_gram(p, 0, k)
                    copy_transposed(p, 1, k // 2)
                copy_transposed(p, 1, TG - 1)
                copy_gram(p, 1, 0)
                copy_gram(p, 1, 2)
                copy_inputs(p, 0)
                copy_gram(p, 1, 4)
                copy_gram(p, 1, 6)

            cast_ids(0)
            for f in range(NOH):
                w = raw[f % 2][:, 0:KT[f], :]
                act.wait_ge(s_raw[f % 2], 16 * (f // 2 + 1))
                act.activation(tab[f][:, 0, :, :], w, ACT.Copy).then_inc(s_hi, 1)
                act.wait_ge(s_rest, f + 1)
                act.activation(tab[f][:, 1, :, :], w, ACT.Copy).then_inc(s_mid, 1)
            act.wait_ge(s_wts, 16 * 6)
            act.wait_ge(s_zero, 1)
            step(0, True, False)
            with act.Fori(1, NPAIR - 1) as p:
                step(p, False, False)
            step(NPAIR - 1, False, True)
            copy_inputs(NPAIR - 1, 1)
            for u in range(4):
                copy_layer(NPAIR - 1, u)

        @block.tensor
        def _(pe):
            def lookup(p, f, first=False):
                pe.wait_ge(s_oh, p * NOH + f + 1)
                if first:
                    pe.wait_ge(s_tab, f + 1)
                wait(pe, s_xf[f % 2], x_onehot(p, f) - 1)
                n = KT[f] * PARTS
                for i in range(n):
                    t, part = divmod(i, PARTS)
                    ins = pe.matmul(xb[f % 2][:, 0:PAIR], tab[f][:, part, t, :], onehot[f][:, t, :],
                                    start=(i == 0), stop=(i == n - 1))
                ins.then_inc(s_x[f % 2], 1)

            def transpose_rows(p, s, g):
                pe.wait_ge(s_rows[s][g], p * 64 + 64)
                wait(pe, s_tf, p * 2 * TG + s * TG + g - 1)
                for j in range(FG):
                    ins = pe.transpose(tb[(s * TG + g) % 2][:, j * P:j * P + P], rows[s][:, FG * g + j, :], ident[:, :])
                ins.then_inc(s_t, 1)

            def gram_products(p, s, k):
                if k == 0:
                    pe.wait_ge(s_tf, p * 2 * TG + s * TG + TG)
                    pe.wait_ge(s_xf[0], x_onehot(p, NOH - 1))
                    pe.wait_ge(s_xf[1], x_onehot(p, NOH - 2))
                wait(pe, s_gf[k % 2], p * 8 + 4 * s + k // 2)
                for j in range(GB):
                    x = emb_g[:, s, GB * k + j, :, :]
                    ins = pe.matmul(gb[k % 2][:, j * 4 * NF:(j + 1) * 4 * NF], x.rearrange("p q f -> p (q f)"), x[:, :, 0:NF],
                                    start=True, stop=True)
                ins.then_inc(s_g, 1)

            def transpose_inputs(p, s):
                pe.wait_ge(s_z, p * 2 + s + 1)
                pe.wait_ge(s_dense[s], p * 16 + 16)
                wait(pe, s_xf[1], x1_inputs(p, s) - 1)
                for c in range(KC):
                    ins = pe.transpose(xb[1][:, c * P:c * P + P], zin[s][:, c * P:c * P + P], ident[:, :])
                ins.then_inc(s_x[1], 1)

            def layer1(p, u):
                pe.wait_ge(s_xf[1], x1_inputs(p, 1))
                for c in (2 * u, 2 * u + 1):
                    for k in range(KC):
                        n = P if k < KC - 1 else LAST
                        ins = pe.matmul(mb[u][:, (c % 2) * PAIR:(c % 2 + 1) * PAIR], w1s[0:n, k, c * P:c * P + P],
                                        h0[0:n, k, :], start=(k == 0), stop=(k == KC - 1))
                ins.then_inc(s_m, 1)

            def layer2(p):
                pe.wait_ge(s_mf, p * 4 + 2)
                for c in range(H2 // P):
                    for k in range(H1 // P):
                        ins = pe.matmul(mb[0][:, c * PAIR:(c + 1) * PAIR], w2s[:, k, c * P:c * P + P], h1[:, k, :],
                                        start=(k == 0), stop=(k == H1 // P - 1))
                ins.then_inc(s_m, 1)

            def layer3(p):
                pe.wait_ge(s_mf, p * 4 + 3)
                for k in range(H2 // P):
                    ins = pe.matmul(mb[1][0:1, 0:PAIR], w3s[:, k:k + 1], h2[:, k, :], start=(k == 0), stop=(k == H2 // P - 1))
                ins.then_inc(s_m, 1)

            def step(p, first):
                lookup(p, 0, first)
                if not first:
                    transpose_inputs(p - 1, 1)
                lookup(p, 1, first)
                if not first:
                    layer1(p - 1, 0)
                    layer1(p - 1, 1)
                lookup(p, 2, first)
                if not first:
                    layer2(p - 1)
                lookup(p, 3, first)
                if not first:
                    layer3(p - 1)
                for g in range(TG):
                    transpose_rows(p, 0, g)
                    if 4 + g < NOH:
                        lookup(p, 4 + g, first)
                for k in range(NGB):
                    gram_products(p, 0, k)
                    if k % 2:
                        transpose_rows(p, 1, k // 2)
                transpose_rows(p, 1, TG - 1)
                for k in range(NGB):
                    if k == NGB // 2:
                        transpose_inputs(p, 0)
                    gram_products(p, 1, k)

            pe.wait_ge(s_ident, 2)
            pe.wait_ge(s_zero, 1)
            pe.wait_ge(s_wts, 16 * 6)
            step(0, True)
            with pe.Fori(1, NPAIR) as p:
                step(p, False)
            q = NPAIR - 1
            transpose_inputs(q, 1)
            layer1(q, 0)
            layer1(q, 1)
            layer2(q)
            layer3(q)


def kernel(**inputs):
    from concourse import bacc
    from concourse.bass_utils import run_bass_kernel_spmd

    ids = np.asarray(inputs["ids"])
    arrays = {"ids": ids, "ids_t": ids[:, ONEHOT].T, "dense": inputs["dense_ctx"],
              "w1": np.asarray(inputs["W_top1"])[first_layer_rows()], "b1": np.asarray(inputs["b_top1"]).reshape(-1, P).T,
              "w2": inputs["W_top2"], "b2": np.asarray(inputs["b_top2"]).reshape(-1, P).T,
              "w3": np.asarray(inputs["W_top3"]).reshape(-1, P).T}
    arrays.update({f"tbl_{f}": inputs[f"tbl_{f}"] for f in range(NF)})
    arrays = {k: np.ascontiguousarray(v) for k, v in arrays.items()}
    nc = bacc.Bacc("TRN2", target_bir_lowering=False, num_devices=1)
    ap = {k: nc.dram_tensor(k, v.shape, mybir.dt.from_np(v.dtype), kind="ExternalInput").ap() for k, v in arrays.items()}
    out = nc.dram_tensor("out", (BATCH, 1), mybir.dt.float32, kind="ExternalOutput").ap()
    dlrm_tower(nc, ap["ids"], ap["ids_t"], ap["dense"], [ap[f"tbl_{f}"] for f in range(NF)],
               ap["w1"], ap["b1"], ap["w2"], ap["b2"], ap["w3"], out)
    result = run_bass_kernel_spmd(nc, [arrays], core_ids=[0])
    return result.results[0]["out"]
```

```python
import numpy as np
import concourse.bass as bass
from concourse import mybir
from contextlib import ExitStack

P = 128
BATCH, NF, D, ND = 2048, 27, 128, 16
ROWS = [1250, 1000, 1250, 1250, 1000, 125000, 1000, 1250, 1000, 1250, 1250, 1250, 1000, 1250, 1250,
        12500, 12500, 1000, 1250, 1250, 1250, 1250, 1250, 12500, 12500, 12500, 1250]
H1, H2 = 512, 256

NOH = 7
ONEHOT = sorted(range(NF), key=lambda f: ROWS[f])[:NOH]
GATHER = [f for f in range(NF) if f not in ONEHOT]
ORDER = GATHER + ONEHOT
NG = len(GATHER)
KR = 125
KT = [ROWS[f] // KR for f in ONEHOT]
PARTS = 2
UPPER = -1 << 12
RING = 4

PAIR = 2 * P
NPAIR = BATCH // PAIR
FG = 4
TG = NG // FG
GATHERED = 16 * FG
FP = 32
GS = P // 4
GB = 4
NGB = GS // GB
HALF = (NF - 1) // 2
NZ = NF * HALF
ZROW = NF + HALF
NIN = NZ + ND
KC = -(-NIN // P)
LAST = NIN - (KC - 1) * P


def first_layer_rows():
    i, j = np.triu_indices(NF, k=1)
    number = {(int(a), int(b)): n for n, (a, b) in enumerate(zip(i, j))}
    rows = []
    for a in range(NF):
        for k in range(1, HALF + 1):
            x, y = ORDER[a], ORDER[(a + k) % NF]
            rows.append(number[min(x, y), max(x, y)])
    return rows + list(range(NZ, NIN))


def wait(eng, sem, value):
    if not isinstance(value, int) or value > 0:
        eng.wait_ge(sem, value)


def dlrm_tower(nc, ids, ids_t, dense, tables, w1, b1, w2, b2, w3, out):
    fp32, fp32r, fp16, i32 = mybir.dt.float32, mybir.dt.float32r, mybir.dt.float16, mybir.dt.int32
    ALU, ACT = mybir.AluOpType, mybir.ActivationFunctionType
    ctx = ExitStack()
    with ctx:
        def sb(name, shape, dt):
            return ctx.enter_context(nc.sbuf_tensor(name, shape, dt))

        def sem(name):
            return ctx.enter_context(nc.semaphore(name))

        rows = [sb(f"rows{s}", [P, NG, D], fp32) for s in range(2)]
        emb = sb("emb", [P, 2 * P * FP], fp32)
        emb_g = emb[:, :].rearrange("p (s g q f) -> p s g q f", s=2, g=GS, q=4)
        emb_w = emb[:, :].rearrange("p (s g q f) -> p s f q g", s=2, g=GS, q=4)
        raw = sb("raw", [KR, 2, max(KT), D], fp32)
        upper = sb("upper", [KR, max(KT), D], fp32)
        tab = [sb(f"tab{f}", [KR, PARTS, KT[f], D], fp32r) for f in range(NOH)]
        onehot = [sb(f"onehot{b}", [KR, max(KT[b::RING]), PAIR], fp32r) for b in range(RING)]
        idx = [sb(f"idx{s}", [P, NF], i32) for s in range(2)]
        idb = sb("idb", [KR, NOH, PAIR], i32)
        idh = sb("idh", [KR, NOH, PAIR], fp16)
        rown_i = sb("rown_i", [KR, sum(sorted(set(KT)))], i32)
        rown = sb("rown", [KR, sum(sorted(set(KT)))], fp32)
        ident = sb("ident", [P, P], fp32)
        gram = [sb(f"gram{s}", [P, GS, NF], fp32) for s in range(2)]
        zrow = sb("zrow", [P, NF, ZROW], fp32)
        zin = [sb(f"zin{s}", [P, KC * P], fp32) for s in range(2)]
        h0 = sb("h0", [P, KC, PAIR], fp32)
        h1 = sb("h1", [P, H1 // P, PAIR], fp32)
        h2 = sb("h2", [P, H2 // P, PAIR], fp32)
        ysb = raw[0:1, :, :, :].rearrange("p s t d -> p (s t d)")[:, 0:BATCH]
        w1s = sb("w1s", [P, KC, H1], fp32)
        w2s = sb("w2s", [P, H1 // P, H2], fp32)
        w3s = sb("w3s", [P, H2 // P], fp32)
        b1s = sb("b1s", [P, H1 // P], fp32)
        b2s = sb("b2s", [P, H2 // P], fp32)

        def bank(name):
            return ctx.enter_context(nc.psum_tensor(name, [P, 512], fp32))

        tb = [bank(f"tb{i}") for i in range(2)]
        gb = [bank(f"gb{i}") for i in range(2)]
        xb = [bank(f"xb{i}") for i in range(2)]
        mb = [bank(f"mb{i}") for i in range(2)]

        s_ident = sem("identity_built")
        s_rowi = sem("row_numbers_built")
        s_rown = sem("row_numbers_cast")
        s_zero = sem("pads_zeroed")
        s_idx = [sem(f"ids_loaded{s}") for s in range(2)]
        s_idb = sem("onehot_ids_loaded")
        s_idh = sem("onehot_ids_cast")
        s_free = sem("rows_free")
        s_oh = sem("onehot_made")
        s_raw = [sem(f"table_loaded{s}") for s in range(2)]
        s_up = sem("table_masked")
        s_tab = sem("table_split")
        s_wts = sem("weights_loaded")
        s_rows = [[sem(f"gathered{s}_{g}") for g in range(TG)] for s in range(2)]
        s_t, s_tf = sem("transposed"), sem("transposed_copied")
        s_g = sem("gram_done")
        s_gf = [sem(f"gram_copied{i}") for i in range(2)]
        s_x = [sem(f"x_done{i}") for i in range(2)]
        s_xf = [sem(f"x_copied{i}") for i in range(2)]
        s_m, s_mf = sem("layer_done"), sem("layer_copied")
        s_zt, s_zd, s_z = sem("products_turned"), sem("products_repeated"), sem("inputs_packed")
        s_dense = [sem(f"dense_loaded{s}") for s in range(2)]
        s_out = sem("out_stored")

        X = [0, 0, 1, 0, 1, 0, 1]

        def x_onehot(p, f):
            return p * (5 if X[f] else 4) + [1, 2, 1, 3, 2, 4, 3][f]

        def x1_inputs(p, s):
            return p * 5 + 4 + s

        tcol = {t: sum(x for x in sorted(set(KT)) if x < t) for t in set(KT)}
        block = ctx.enter_context(nc.Block())

        @block.sync
        def _(sp):
            def load_ids(p, s):
                sp.dma_start(idx[s][:, :], ids[bass.ds((p * 2 + s) * P, P), :]).then_inc(s_idx[s], 16)

            def load_onehot_ids(p):
                src = ids_t[:, bass.ds(p * PAIR, PAIR)].rearrange("(o f) b -> o f b", o=1).to_broadcast([KR, NOH, PAIR])
                sp.dma_start(idb[:, :, :], src).then_inc(s_idb, 16)

            def load_dense(p, s):
                wait(sp, s_x[1], x1_inputs(p - 1, s))
                sp.dma_start(zin[s][:, NZ:NIN], dense[bass.ds((p * 2 + s) * P, P), :]).then_inc(s_dense[s], 16)

            def step(p, last):
                load_dense(p, 0)
                if not last:
                    sp.wait_ge(s_idh, p + 1)
                    load_onehot_ids(p + 1)
                    for g in range(TG):
                        sp.wait_ge(s_rows[0][g], (p + 1) * GATHERED)
                    load_ids(p + 1, 0)
                load_dense(p, 1)
                if not last:
                    for g in range(TG):
                        sp.wait_ge(s_rows[1][g], (p + 1) * GATHERED)
                    load_ids(p + 1, 1)

            load_ids(0, 0)
            load_ids(0, 1)
            load_onehot_ids(0)
            for f in range(NOH):
                if f >= 2:
                    sp.wait_ge(s_tab, 2 * f - 2)
                src = tables[ONEHOT[f]].rearrange("(p t) d -> p t d", t=KT[f])
                sp.dma_start(raw[:, f % 2, 0:KT[f], :], src).then_inc(s_raw[f % 2], 16)
            sp.dma_start(w1s[:, 0:KC - 1, :], w1[0:(KC - 1) * P, :].rearrange("(c p) n -> p c n", p=P)).then_inc(s_wts, 16)
            sp.dma_start(w1s[0:LAST, KC - 1, :], w1[(KC - 1) * P:NIN, :]).then_inc(s_wts, 16)
            sp.dma_start(w2s[:, :, :], w2.rearrange("(c p) n -> p c n", p=P)).then_inc(s_wts, 16)
            sp.dma_start(w3s[:, :], w3).then_inc(s_wts, 16)
            sp.dma_start(b1s[:, :], b1).then_inc(s_wts, 16)
            sp.dma_start(b2s[:, :], b2).then_inc(s_wts, 16)
            step(0, False)
            with sp.Fori(1, NPAIR - 1) as p:
                step(p, False)
            step(NPAIR - 1, True)
            sp.wait_ge(s_mf, 4 * NPAIR)
            sp.dma_start(out.rearrange("b o -> o b"), ysb[:, :]).then_inc(s_out, 16)
            sp.wait_ge(s_out, 16)

        @block.gpsimd
        def _(pool):
            def gather(p, s):
                pool.wait_ge(s_idx[s], p * 16 + 16)
                for g in range(TG):
                    wait(pool, s_t, (p - 1) * 2 * TG + s * TG + g + 1)
                    pool.sem_inc(s_free, 1)
                    for j in range(FG * g, FG * g + FG):
                        f = GATHER[j]
                        pool.indirect_dma_start(
                            out=rows[s][:, j, :], out_offset=None, in_=tables[f][:, :],
                            in_offset=bass.IndirectOffsetOnAxis(ap=idx[s][:, f:f + 1], axis=0),
                        ).then_inc(s_rows[s][g], 16)

            for t in sorted(set(KT)):
                pool.iota(rown_i[:, tcol[t]:tcol[t] + t], pattern=[[1, t]], base=0, channel_multiplier=t).then_inc(s_rowi, 1)
            pool.memset(ident[:, :], 0.0).then_inc(s_ident, 1)
            pool.wait_ge(s_ident, 1)
            pool.affine_select(out=ident[:, :], in_=ident[:, :], compare_op=ALU.not_equal, fill=1.0, base=0,
                               pattern=[[-1, P]], channel_multiplier=1).then_inc(s_ident, 1)
            for s in range(2):
                gather(0, s)
            with pool.Fori(1, NPAIR) as p:
                for s in range(2):
                    gather(p, s)

        @block.vector
        def _(dve):
            def split_table(f):
                w, u = raw[:, f % 2, 0:KT[f], :], upper[:, 0:KT[f], :]
                dve.wait_ge(s_raw[f % 2], 16 * (f // 2 + 1))
                wait(dve, s_tab, 2 * f)
                dve.tensor_scalar(u.bitcast(i32), w.bitcast(i32), UPPER, None, ALU.bitwise_and).then_inc(s_up, 1)
                dve.wait_ge(s_up, f + 1)
                dve.tensor_tensor(tab[f][:, 1, :, :], w, u, ALU.subtract).then_inc(s_tab, 1)
                dve.tensor_copy(tab[f][:, 0, :, :], u).then_inc(s_tab, 1)

            def make_onehot(p, f):
                if f == 0:
                    dve.wait_ge(s_idh, p + 1)
                if f >= RING:
                    dve.wait_ge(s_x[X[f - RING]], x_onehot(p, f - RING))
                else:
                    before = f + RING if f + RING < NOH else f
                    wait(dve, s_x[X[before]], x_onehot(p - 1, before))
                for t in range(KT[f]):
                    ins = dve.tensor_scalar(onehot[f % RING][:, t, :], idh[:, f, :],
                                            rown[:, tcol[KT[f]] + t:tcol[KT[f]] + t + 1], None, ALU.is_equal)
                ins.then_inc(s_oh, 1)

            def copy_gram(p, s, k):
                dve.wait_ge(s_g, p * 16 + s * NGB + k + 1)
                if k == 1:
                    wait(dve, s_zt, (p - 1) * 2 + s + 1)
                for q in range(4):
                    ins = dve.tensor_copy(
                        gram[s][32 * q:32 * q + 32, GB * k:GB * k + GB, :],
                        gb[1][32 * q:32 * q + 32, 0:GB * 4 * NF].rearrange("p (g c) -> p g c", g=GB)[:, :, NF * q:NF * q + NF])
                ins.then_inc(s_gf[1], 1)

            def pack_inputs(p, s):
                n = p * 2 + s
                dve.wait_ge(s_gf[0], p * 8 + 4 * s + 4)
                dve.wait_ge(s_gf[1], p * 8 + 4 * s + 4)
                wait(dve, s_z, n)
                dve.transpose(zrow[:, :, 0:FP], gram[s][:, :, :].rearrange("p g f -> p f g")).then_inc(s_zt, 1)
                dve.wait_ge(s_zt, n + 1)
                dve.tensor_copy(zrow[:, HALF + 1:NF, NF:ZROW], zrow[:, HALF + 1:NF, 0:HALF]).then_inc(s_zd, 1)
                dve.wait_ge(s_zd, n + 1)
                wait(dve, s_x[1], x1_inputs(p - 1, s))
                flat = zrow[:, :, :].rearrange("p a c -> p (a c)")
                diagonal = bass.AP(tensor=flat.tensor, offset=flat.offset + 1,
                                   ap=[list(flat.ap[0]), [ZROW + 1, NF], [1, HALF]])
                dve.tensor_copy(zin[s][:, 0:NZ].rearrange("p (a k) -> p a k", a=NF), diagonal).then_inc(s_z, 1)

            def step(p, first, last):
                if not first:
                    for f in range(RING, NOH):
                        make_onehot(p, f)
                if not last:
                    make_onehot(p + 1, 0)
                    make_onehot(p + 1, 1)
                for s in range(2):
                    for k in range(1, NGB, 2):
                        copy_gram(p, s, k)
                    pack_inputs(p, s)
                if not last:
                    make_onehot(p + 1, 2)
                    make_onehot(p + 1, 3)

            for s in range(2):
                dve.memset(zin[s][:, NIN:KC * P], 0.0)
            dve.memset(emb[:, :].rearrange("p (b f) -> p b f", f=FP)[:, :, NF:FP], 0.0).then_inc(s_zero, 1)
            dve.wait_ge(s_rowi, len(set(KT)))
            dve.tensor_copy(rown[:, :], rown_i[:, :]).then_inc(s_rown, 1)
            dve.wait_ge(s_rown, 1)
            for f in range(NOH):
                if f < RING:
                    make_onehot(0, f)
                split_table(f)
                if f >= RING:
                    make_onehot(0, f)
            step(0, True, False)
            with dve.Fori(1, NPAIR - 1) as p:
                step(p, False, False)
            step(NPAIR - 1, False, True)

        @block.scalar
        def _(act):
            def cast_ids(p):
                act.wait_ge(s_idb, p * 16 + 16)
                wait(act, s_oh, p * NOH)
                act.activation(idh[:, :, :], idb[:, :, :], ACT.Copy).then_inc(s_idh, 1)

            def copy_onehot(p, f):
                act.wait_ge(s_x[X[f]], x_onehot(p, f))
                if f == 0:
                    wait(act, s_g, p * 16)
                act.activation(emb_w[:, :, NG + f, :, :], xb[X[f]][:, 0:PAIR].rearrange("p (s q g) -> p s q g", s=2, q=4),
                               ACT.Copy).then_inc(s_xf[X[f]], 1)

            def copy_transposed(p, s, g):
                act.wait_ge(s_t, p * 2 * TG + s * TG + g + 1)
                act.activation(emb_w[:, s, FG * g:FG * g + FG, :, :],
                               tb[(s * TG + g) % 2][:, 0:FG * P].rearrange("p (f q b) -> p f q b", f=FG, q=4), ACT.Copy).then_inc(s_tf, 1)

            def copy_gram(p, s, k):
                act.wait_ge(s_g, p * 16 + s * NGB + k + 1)
                if k == 0:
                    wait(act, s_zt, (p - 1) * 2 + s + 1)
                for q in range(4):
                    ins = act.activation(
                        gram[s][32 * q:32 * q + 32, GB * k:GB * k + GB, :],
                        gb[0][32 * q:32 * q + 32, 0:GB * 4 * NF].rearrange("p (g c) -> p g c", g=GB)[:, :, NF * q:NF * q + NF],
                        ACT.Copy)
                ins.then_inc(s_gf[0], 1)

            def copy_inputs(p, s):
                act.wait_ge(s_x[1], x1_inputs(p, s))
                if s == 0:
                    wait(act, s_m, p * 4 - 2)
                act.activation(h0[:, :, s * P:s * P + P], xb[1][:, 0:KC * P].rearrange("p (c b) -> p c b", c=KC),
                               ACT.Copy).then_inc(s_xf[1], 1)

            def copy_layer(p, u):
                act.wait_ge(s_m, p * 4 + u + 1)
                if u < 2:
                    for c in range(2):
                        ins = act.activation(h1[:, 2 * u + c, :], mb[u][:, c * PAIR:c * PAIR + PAIR], ACT.Relu,
                                             bias=b1s[:, 2 * u + c:2 * u + c + 1])
                elif u == 2:
                    for c in range(2):
                        ins = act.activation(h2[:, c, :], mb[0][:, c * PAIR:c * PAIR + PAIR], ACT.Relu, bias=b2s[:, c:c + 1])
                else:
                    ins = act.activation(ysb[:, bass.ds(p * PAIR, PAIR)], mb[1][0:1, 0:PAIR], ACT.Copy)
                ins.then_inc(s_mf, 1)

            def step(p, first, last):
                copy_onehot(p, 0)
                copy_transposed(p, 0, 0)
                copy_transposed(p, 0, 1)
                copy_onehot(p, 1)
                if not first:
                    copy_inputs(p - 1, 1)
                copy_transposed(p, 0, 2)
                copy_onehot(p, 2)
                if not first:
                    copy_layer(p - 1, 0)
                    copy_layer(p - 1, 1)
                copy_onehot(p, 3)
                if not first:
                    copy_layer(p - 1, 2)
                copy_transposed(p, 0, 3)
                if not last and not first:
                    cast_ids(p + 1)
                copy_onehot(p, 4)
                if not first:
                    copy_layer(p - 1, 3)
                copy_transposed(p, 0, 4)
                copy_onehot(p, 5)
                if first:
                    cast_ids(p + 1)
                copy_onehot(p, 6)
                copy_transposed(p, 1, 0)
                copy_transposed(p, 1, 1)
                for k in range(0, NGB, 2):
                    copy_gram(p, 0, k)
                    if k < NGB - 2:
                        copy_transposed(p, 1, 2 + k // 2)
                for k in range(0, NGB, 2):
                    copy_gram(p, 1, k)
                    if k == NGB // 2:
                        copy_inputs(p, 0)

            cast_ids(0)
            act.wait_ge(s_zero, 1)
            step(0, True, False)
            with act.Fori(1, NPAIR - 1) as p:
                step(p, False, False)
            step(NPAIR - 1, False, True)
            copy_inputs(NPAIR - 1, 1)
            for u in range(4):
                copy_layer(NPAIR - 1, u)

        @block.tensor
        def _(pe):
            def lookup(p, f, first=False):
                pe.wait_ge(s_oh, p * NOH + f + 1)
                if first:
                    pe.wait_ge(s_tab, 2 * f + 2)
                wait(pe, s_xf[X[f]], x_onehot(p, f) - 1)
                n = KT[f] * PARTS
                for i in range(n):
                    t, part = divmod(i, PARTS)
                    ins = pe.matmul(xb[X[f]][:, 0:PAIR], tab[f][:, part, t, :], onehot[f % RING][:, t, :],
                                    start=(i == 0), stop=(i == n - 1))
                ins.then_inc(s_x[X[f]], 1)

            def transpose_rows(p, s, g):
                pe.wait_ge(s_rows[s][g], (p + 1) * GATHERED)
                wait(pe, s_tf, p * 2 * TG + s * TG + g - 1)
                for j in range(FG):
                    ins = pe.transpose(tb[(s * TG + g) % 2][:, j * P:j * P + P], rows[s][:, FG * g + j, :], ident[:, :])
                ins.then_inc(s_t, 1)

            def gram_products(p, s, k):
                if k == 0:
                    pe.wait_ge(s_tf, p * 2 * TG + s * TG + TG)
                    pe.wait_ge(s_xf[X[NOH - 2]], x_onehot(p, NOH - 2))
                    pe.wait_ge(s_xf[X[NOH - 1]], x_onehot(p, NOH - 1))
                wait(pe, s_gf[k % 2], p * 8 + 4 * s + k // 2)
                for j in range(GB):
                    x = emb_g[:, s, GB * k + j, :, :]
                    ins = pe.matmul(gb[k % 2][:, j * 4 * NF:(j + 1) * 4 * NF], x.rearrange("p q f -> p (q f)"), x[:, :, 0:NF],
                                    start=True, stop=True)
                ins.then_inc(s_g, 1)

            def transpose_inputs(p, s):
                pe.wait_ge(s_z, p * 2 + s + 1)
                pe.wait_ge(s_dense[s], p * 16 + 16)
                wait(pe, s_xf[1], x1_inputs(p, s) - 1)
                for c in range(KC):
                    ins = pe.transpose(xb[1][:, c * P:c * P + P], zin[s][:, c * P:c * P + P], ident[:, :])
                ins.then_inc(s_x[1], 1)

            def layer1(p, u):
                pe.wait_ge(s_xf[1], x1_inputs(p, 1))
                for c in (2 * u, 2 * u + 1):
                    for k in range(KC):
                        n = P if k < KC - 1 else LAST
                        ins = pe.matmul(mb[u][:, (c % 2) * PAIR:(c % 2 + 1) * PAIR], w1s[0:n, k, c * P:c * P + P],
                                        h0[0:n, k, :], start=(k == 0), stop=(k == KC - 1))
                ins.then_inc(s_m, 1)

            def layer2(p):
                pe.wait_ge(s_mf, p * 4 + 2)
                for c in range(H2 // P):
                    for k in range(H1 // P):
                        ins = pe.matmul(mb[0][:, c * PAIR:(c + 1) * PAIR], w2s[:, k, c * P:c * P + P], h1[:, k, :],
                                        start=(k == 0), stop=(k == H1 // P - 1))
                ins.then_inc(s_m, 1)

            def layer3(p):
                pe.wait_ge(s_mf, p * 4 + 3)
                for k in range(H2 // P):
                    ins = pe.matmul(mb[1][0:1, 0:PAIR], w3s[:, k:k + 1], h2[:, k, :], start=(k == 0), stop=(k == H2 // P - 1))
                ins.then_inc(s_m, 1)

            def step(p, first):
                lookup(p, 0, first)
                transpose_rows(p, 0, 0)
                transpose_rows(p, 0, 1)
                lookup(p, 1, first)
                if not first:
                    transpose_inputs(p - 1, 1)
                transpose_rows(p, 0, 2)
                lookup(p, 2, first)
                if not first:
                    layer1(p - 1, 0)
                    layer1(p - 1, 1)
                lookup(p, 3, first)
                if not first:
                    layer2(p - 1)
                transpose_rows(p, 0, 3)
                lookup(p, 4, first)
                if not first:
                    layer3(p - 1)
                transpose_rows(p, 0, 4)
                lookup(p, 5, first)
                lookup(p, 6, first)
                transpose_rows(p, 1, 0)
                transpose_rows(p, 1, 1)
                for k in range(NGB):
                    gram_products(p, 0, k)
                    if k in (1, 3, 5):
                        transpose_rows(p, 1, 2 + k // 2)
                for k in range(NGB):
                    gram_products(p, 1, k)
                    if k == NGB // 2:
                        transpose_inputs(p, 0)

            pe.wait_ge(s_ident, 2)
            pe.wait_ge(s_zero, 1)
            step(0, True)
            pe.wait_ge(s_wts, 16 * 6)
            with pe.Fori(1, NPAIR) as p:
                step(p, False)
            q = NPAIR - 1
            transpose_inputs(q, 1)
            layer1(q, 0)
            layer1(q, 1)
            layer2(q)
            layer3(q)


def kernel(**inputs):
    from concourse import bacc
    from concourse.bass_utils import run_bass_kernel_spmd

    ids = np.asarray(inputs["ids"])
    arrays = {"ids": ids, "ids_t": ids[:, ONEHOT].T, "dense": inputs["dense_ctx"],
              "w1": np.asarray(inputs["W_top1"])[first_layer_rows()], "b1": np.asarray(inputs["b_top1"]).reshape(-1, P).T,
              "w2": inputs["W_top2"], "b2": np.asarray(inputs["b_top2"]).reshape(-1, P).T,
              "w3": np.asarray(inputs["W_top3"]).reshape(-1, P).T}
    arrays.update({f"tbl_{f}": inputs[f"tbl_{f}"] for f in range(NF)})
    arrays = {k: np.ascontiguousarray(v) for k, v in arrays.items()}
    nc = bacc.Bacc("TRN2", target_bir_lowering=False, num_devices=1)
    ap = {k: nc.dram_tensor(k, v.shape, mybir.dt.from_np(v.dtype), kind="ExternalInput").ap() for k, v in arrays.items()}
    out = nc.dram_tensor("out", (BATCH, 1), mybir.dt.float32, kind="ExternalOutput").ap()
    dlrm_tower(nc, ap["ids"], ap["ids_t"], ap["dense"], [ap[f"tbl_{f}"] for f in range(NF)],
               ap["w1"], ap["b1"], ap["w2"], ap["b2"], ap["w3"], out)
    result = run_bass_kernel_spmd(nc, [arrays], core_ids=[0])
    return result.results[0]["out"]
```

```python
import numpy as np
import concourse.bass as bass
from concourse import mybir
from contextlib import ExitStack

P = 128
BATCH, NF, D, ND = 2048, 27, 128, 16
ROWS = [1250, 1000, 1250, 1250, 1000, 125000, 1000, 1250, 1000, 1250, 1250, 1250, 1000, 1250, 1250,
        12500, 12500, 1000, 1250, 1250, 1250, 1250, 1250, 12500, 12500, 12500, 1250]
H1, H2 = 512, 256

NOH = 7
ONEHOT = sorted(range(NF), key=lambda f: ROWS[f])[:NOH]
GATHER = [f for f in range(NF) if f not in ONEHOT]
ORDER = GATHER + ONEHOT
NG = len(GATHER)
KR = 125
KT = [ROWS[f] // KR for f in ONEHOT]
PARTS = 2
UPPER = -1 << 12
RING = 4
ACT_MADE = (2, 5)

EARLY = 2
PAIR = 2 * P
NPAIR = BATCH // PAIR
FG = 4
TG = NG // FG
GATHERED = 16 * FG
FP = 32
GROWS = 3 * FP + NF
GS = P // 4
GB = 4
NGB = GS // GB
HALF = (NF - 1) // 2
NZ = NF * HALF
ZROW = NF + HALF
NIN = NZ + ND
KC = -(-NIN // P)
LAST = NIN - (KC - 1) * P


def first_layer_rows():
    i, j = np.triu_indices(NF, k=1)
    number = {(int(a), int(b)): n for n, (a, b) in enumerate(zip(i, j))}
    rows = []
    for a in range(NF):
        for k in range(1, HALF + 1):
            x, y = ORDER[a], ORDER[(a + k) % NF]
            rows.append(number[min(x, y), max(x, y)])
    return rows + list(range(NZ, NIN))


def wait(eng, sem, value):
    if not isinstance(value, int) or value > 0:
        eng.wait_ge(sem, value)


def dlrm_tower(nc, ids, ids_t, dense, tables, w1, b1, w2, b2, w3, out):
    fp32, fp32r, fp16, i32 = mybir.dt.float32, mybir.dt.float32r, mybir.dt.float16, mybir.dt.int32
    ALU, ACT = mybir.AluOpType, mybir.ActivationFunctionType
    ctx = ExitStack()
    with ctx:
        def sb(name, shape, dt):
            return ctx.enter_context(nc.sbuf_tensor(name, shape, dt))

        def sem(name):
            return ctx.enter_context(nc.semaphore(name))

        rows = [sb(f"rows{s}", [P, NG, D], fp32) for s in range(2)]
        emb = sb("emb", [P, 2 * P * FP], fp32)
        emb_g = emb[:, :].rearrange("p (s g q f) -> p s g q f", s=2, g=GS, q=4)
        emb_w = emb[:, :].rearrange("p (s g q f) -> p s f q g", s=2, g=GS, q=4)
        raw = sb("raw", [KR, 2, max(KT), D], fp32)
        upper = sb("upper", [KR, max(KT), D], fp32)
        tab = [sb(f"tab{f}", [KR, PARTS, KT[f], D], fp32r) for f in range(NOH)]
        onehot = [sb(f"onehot{b}", [KR, max(KT[b::RING]), PAIR], fp32r) for b in range(RING)]
        idx = [sb(f"idx{s}", [P, NF], i32) for s in range(2)]
        idb = sb("idb", [KR, NOH, PAIR], i32)
        idh = sb("idh", [KR, NOH, PAIR], fp16)
        rown_i = sb("rown_i", [KR, sum(sorted(set(KT)))], i32)
        one = sb("one", [KR, 1], fp32)
        rown = sb("rown", [KR, sum(sorted(set(KT)))], fp32)
        ident = sb("ident", [P, P], fp32)
        gram = [sb(f"gram{s}", [P, GS, NF], fp32) for s in range(2)]
        zrow = sb("zrow", [P, NF, ZROW], fp32)
        upper_odd = zrow[0:KR, :, :].rearrange("p a c -> p (a c)")[:, 0:max(KT[1::2]) * D].rearrange("p (t d) -> p t d", d=D)
        zin = [sb(f"zin{s}", [P, KC * P], fp32) for s in range(2)]
        h0 = sb("h0", [P, KC, PAIR], fp32)
        h1 = sb("h1", [P, H1 // P, PAIR], fp32)
        h2 = sb("h2", [P, H2 // P, PAIR], fp32)
        ysb = raw[0:1, :, :, :].rearrange("p s t d -> p (s t d)")[:, 0:BATCH]
        w1s = sb("w1s", [P, KC, H1], fp32)
        w2s = sb("w2s", [P, H1 // P, H2], fp32)
        w3s = sb("w3s", [P, H2 // P], fp32)
        squares = [h1, w2s]
        b1s = sb("b1s", [P, H1 // P], fp32)
        b2s = sb("b2s", [P, H2 // P], fp32)

        def bank(name):
            return ctx.enter_context(nc.psum_tensor(name, [P, 512], fp32))

        tb = [bank(f"tb{i}") for i in range(2)]
        gb = [bank(f"gb{i}") for i in range(2)]
        xb = [bank(f"xb{i}") for i in range(2)]
        mb = [bank(f"mb{i}") for i in range(2)]
        lb = gb + tb

        s_ident = sem("identity_built")
        s_rowi = sem("row_numbers_built")
        s_rown = sem("row_numbers_cast")
        s_zero = sem("pads_zeroed")
        s_idx = [sem(f"ids_loaded{s}") for s in range(2)]
        s_early = sem("early_onehot_ids_loaded")
        s_idb = sem("onehot_ids_loaded")
        s_idh = sem("onehot_ids_cast")
        s_free = sem("rows_free")
        s_oh = sem("onehot_made")
        s_sq = sem("squares_made")
        s_oha = sem("onehot_made_act")
        s_raw = [sem(f"table_loaded{s}") for s in range(2)]
        s_up = sem("table_masked")
        s_rest = sem("table_rest_made")
        s_upc = sem("table_upper_copied")
        s_wts = sem("weights_loaded")
        s_rows = [[sem(f"gathered{s}_{g}") for g in range(TG)] for s in range(2)]
        s_t, s_tf = sem("transposed"), sem("transposed_copied")
        s_g = sem("gram_done")
        s_gf = [sem(f"gram_copied{i}") for i in range(2)]
        s_x = [sem(f"x_done{i}") for i in range(2)]
        s_xf = [sem(f"x_copied{i}") for i in range(2)]
        s_m, s_mf = sem("layer_done"), sem("layer_copied")
        s_l, s_la, s_lv = sem("tile_layer_done"), sem("tile_layer_copied_act"), sem("tile_layer_copied_dve")
        s_zt, s_zd, s_z = sem("products_turned"), sem("products_repeated"), sem("inputs_packed")
        s_dense = [sem(f"dense_loaded{s}") for s in range(2)]
        s_out = sem("out_stored")

        X = [0, 1, 0, 0, 1, 0, 1]

        def x_onehot(p, f):
            if X[f] == 0:
                return p * 4 + {0: 1, 2: 2, 3: 3, 5: 4}[f]
            if f == 1:
                return 1 if isinstance(p, int) and p == 0 else p * 5
            return p * 5 + {4: 2, 6: 3}[f]

        def x1_inputs(p, s):
            if s == 1 and isinstance(p, int) and p == NPAIR - 1:
                return p * 5 + 5
            return p * 5 + (6 if s else 4)

        def made(p, f):
            if isinstance(p, int) and p == 0:
                return sum(x not in ACT_MADE for x in range(f + 1))
            return p * NOH + [2, 3, 4, 1, 5, 6, 7][f] - len(ACT_MADE)

        def upper_part(f):
            return (upper_odd if f % 2 else upper)[:, 0:KT[f], :]

        tcol = {t: sum(x for x in sorted(set(KT)) if x < t) for t in set(KT)}
        block = ctx.enter_context(nc.Block())

        @block.sync
        def _(sp):
            def load_ids(p, s):
                sp.dma_start(idx[s][:, :], ids[bass.ds((p * 2 + s) * P, P), :]).then_inc(s_idx[s], 16)

            def load_onehot_ids(p, f0=0, f1=NOH, signal=s_idb):
                src = ids_t[f0:f1, bass.ds(p * PAIR, PAIR)].rearrange("(o f) b -> o f b", o=1)
                sp.dma_start(idb[:, f0:f1, :], src.to_broadcast([KR, f1 - f0, PAIR])).then_inc(signal, 16)

            def load_dense(p, s):
                wait(sp, s_x[1], x1_inputs(p - 1, s))
                sp.dma_start(zin[s][:, NZ:NIN], dense[bass.ds((p * 2 + s) * P, P), :]).then_inc(s_dense[s], 16)

            def step(p, first, last):
                load_dense(p, 0)
                if not last:
                    if not first:
                        sp.wait_ge(s_idh, p + 2)
                        load_onehot_ids(p + 1)
                    for g in range(TG):
                        sp.wait_ge(s_rows[0][g], (p + 1) * GATHERED)
                    load_ids(p + 1, 0)
                load_dense(p, 1)
                if not last:
                    for g in range(TG):
                        sp.wait_ge(s_rows[1][g], (p + 1) * GATHERED)
                    load_ids(p + 1, 1)

            def load_table(f):
                if f >= 2:
                    sp.wait_ge(s_rest, f - 1)
                src = tables[ONEHOT[f]].rearrange("(p t) d -> p t d", t=KT[f])
                sp.dma_start(raw[:, f % 2, 0:KT[f], :], src).then_inc(s_raw[f % 2], 16)

            load_ids(0, 0)
            load_table(0)
            load_onehot_ids(0, 0, EARLY, s_early)
            load_table(1)
            load_onehot_ids(0, EARLY, NOH)
            load_ids(0, 1)
            for f in range(2, NOH):
                load_table(f)
            sp.wait_ge(s_idh, 2)
            load_onehot_ids(1)
            sp.dma_start(w1s[:, 0:KC - 1, :], w1[0:(KC - 1) * P, :].rearrange("(c p) n -> p c n", p=P)).then_inc(s_wts, 16)
            sp.dma_start(w1s[0:LAST, KC - 1, :], w1[(KC - 1) * P:NIN, :]).then_inc(s_wts, 16)
            sp.wait_ge(s_oha, len(ACT_MADE))
            sp.dma_start(w2s[:, :, :], w2.rearrange("(c p) n -> p c n", p=P)).then_inc(s_wts, 16)
            sp.dma_start(w3s[:, :], w3).then_inc(s_wts, 16)
            sp.dma_start(b1s[:, :], b1).then_inc(s_wts, 16)
            sp.dma_start(b2s[:, :], b2).then_inc(s_wts, 16)
            step(0, True, False)
            with sp.Fori(1, NPAIR - 1) as p:
                step(p, False, False)
            step(NPAIR - 1, False, True)
            sp.wait_ge(s_mf, 4 * (NPAIR - 1))
            sp.wait_ge(s_la, 6)
            sp.dma_start(out.rearrange("b o -> o b"), ysb[:, :]).then_inc(s_out, 16)
            sp.wait_ge(s_out, 16)

        @block.gpsimd
        def _(pool):
            def gather(p, s):
                pool.wait_ge(s_idx[s], p * 16 + 16)
                for g in range(TG):
                    wait(pool, s_t, (p - 1) * 2 * TG + s * TG + g + 1)
                    pool.sem_inc(s_free, 1)
                    for j in range(FG * g, FG * g + FG):
                        f = GATHER[j]
                        pool.indirect_dma_start(
                            out=rows[s][:, j, :], out_offset=None, in_=tables[f][:, :],
                            in_offset=bass.IndirectOffsetOnAxis(ap=idx[s][:, f:f + 1], axis=0),
                        ).then_inc(s_rows[s][g], 16)

            for t in sorted(set(KT)):
                pool.iota(rown_i[:, tcol[t]:tcol[t] + t], pattern=[[1, t]], base=0, channel_multiplier=t).then_inc(s_rowi, 1)
            pool.memset(ident[:, :], 0.0).then_inc(s_ident, 1)
            pool.wait_ge(s_ident, 1)
            pool.affine_select(out=ident[:, :], in_=ident[:, :], compare_op=ALU.not_equal, fill=1.0, base=0,
                               pattern=[[-1, P]], channel_multiplier=1).then_inc(s_ident, 1)
            for s in range(2):
                gather(0, s)
            with pool.Fori(1, NPAIR) as p:
                for s in range(2):
                    gather(p, s)

        @block.vector
        def _(dve):
            def split_table(f):
                w, u = raw[:, f % 2, 0:KT[f], :], upper_part(f)
                dve.wait_ge(s_raw[f % 2], 16 * (f // 2 + 1))
                wait(dve, s_rest, f - 1)
                wait(dve, s_upc, f - 1)
                dve.tensor_scalar(u.bitcast(i32), w.bitcast(i32), UPPER, None, ALU.bitwise_and).then_inc(s_up, 1)
                dve.wait_ge(s_up, f + 1)
                dve.tensor_tensor(tab[f][:, 1, :, :], w, u, ALU.subtract).then_inc(s_rest, 1)

            def make_onehot(p, f, part=None):
                if isinstance(p, int) and p == 0:
                    dve.wait_ge(s_idh, 1 if f < EARLY else 2)
                elif f == 3:
                    dve.wait_ge(s_idh, p + 2)
                if f >= RING:
                    dve.wait_ge(s_x[X[f - RING]], x_onehot(p, f - RING))
                else:
                    before = f + RING if f + RING < NOH else f
                    wait(dve, s_x[X[before]], x_onehot(p - 1, before))
                cut = KT[f] // 2
                for t in (range(KT[f]) if part is None else range(cut) if part == 0 else range(cut, KT[f])):
                    ins = dve.tensor_scalar(onehot[f % RING][:, t, :], idh[:, f, :],
                                            rown[:, tcol[KT[f]] + t:tcol[KT[f]] + t + 1], None, ALU.is_equal)
                if part != 0:
                    ins.then_inc(s_oh, 1)

            def copy_gram(p, s, k):
                dve.wait_ge(s_g, p * 16 + s * NGB + k + 1)
                if k == 1:
                    wait(dve, s_zt, (p - 1) * 2 + s + 1)
                for q in range(4):
                    end = min(FP * q + FP, GROWS)
                    ins = dve.tensor_copy(
                        gram[s][FP * q:end, GB * k:GB * k + GB, :],
                        gb[1][FP * q:end, 0:GB * 4 * NF].rearrange("p (g c) -> p g c", g=GB)[:, :, NF * q:NF * q + NF])
                ins.then_inc(s_gf[1], 1)

            def pack_inputs(p, s):
                n = p * 2 + s
                dve.wait_ge(s_gf[0], p * 8 + 4 * s + 4)
                dve.wait_ge(s_gf[1], p * 8 + 4 * s + 4)
                wait(dve, s_z, n)
                dve.transpose(zrow[:, :, 0:FP], gram[s][:, :, :].rearrange("p g f -> p f g")).then_inc(s_zt, 1)
                dve.wait_ge(s_zt, n + 1)
                dve.tensor_copy(zrow[:, HALF + 1:NF, NF:ZROW], zrow[:, HALF + 1:NF, 0:HALF]).then_inc(s_zd, 1)
                dve.wait_ge(s_zd, n + 1)
                wait(dve, s_x[1], x1_inputs(p - 1, s))
                flat = zrow[:, :, :].rearrange("p a c -> p (a c)")
                diagonal = bass.AP(tensor=flat.tensor, offset=flat.offset + 1,
                                   ap=[list(flat.ap[0]), [ZROW + 1, NF], [1, HALF]])
                dve.tensor_copy(zin[s][:, 0:NZ].rearrange("p (a k) -> p a k", a=NF), diagonal).then_inc(s_z, 1)

            def step(p, first, last):
                if not first:
                    for f in range(RING, NOH):
                        make_onehot(p, f)
                if not last:
                    make_onehot(p + 1, 3)
                    if not first:
                        for f in range(3):
                            make_onehot(p + 1, f)
                for s in range(2):
                    for k in range(1, NGB, 2):
                        copy_gram(p, s, k)
                        n = s * (NGB // 2) + k // 2
                        if first and n in (0, 1, 4, 5, 6, 7):
                            make_onehot(p + 1, {0: 0, 1: 0, 4: 1, 5: 1, 6: 2, 7: 2}[n], n % 2)
                    pack_inputs(p, s)

            dve.memset(one[:, :], 1.0).then_inc(s_zero, 1)
            for s in range(2):
                dve.memset(zin[s][:, NIN:KC * P], 0.0)
                dve.memset(gram[s][3 * FP:P, :, :], 0.0).then_inc(s_zero, 1)
            dve.memset(emb[:, :].rearrange("p (b f) -> p b f", f=FP)[:, :, NF:FP], 0.0).then_inc(s_zero, 1)
            dve.wait_ge(s_rown, 1)
            for f in range(NOH):
                split_table(f)
                if f not in ACT_MADE:
                    make_onehot(0, f)
            step(0, True, False)
            with dve.Fori(1, NPAIR - 1) as p:
                step(p, False, False)
            step(NPAIR - 1, False, True)
            for c in (1, 3):
                dve.wait_ge(s_l, 4 + c)
                dve.tensor_scalar(h1[:, c, P:PAIR], lb[c][:, 0:P], b1s[:, c:c + 1], 0.0, ALU.add, ALU.max).then_inc(s_lv, 1)
            dve.wait_ge(s_l, 9)
            dve.tensor_scalar(h2[:, 1, P:PAIR], mb[1][:, 0:P], b2s[:, 1:2], 0.0, ALU.add, ALU.max).then_inc(s_lv, 1)

        @block.scalar
        def _(act):
            def cast_ids(p, f0=0, f1=NOH):
                if f1 < NOH:
                    act.wait_ge(s_early, 16)
                else:
                    act.wait_ge(s_idb, p * 16 + 16)
                if not isinstance(p, int) or p > 0:
                    act.wait_ge(s_oh, made(p - 1, NOH - 1))
                act.activation(idh[:, f0:f1, :], idb[:, f0:f1, :], ACT.Copy).then_inc(s_idh, 1)

            def copy_onehot(p, f):
                act.wait_ge(s_x[X[f]], x_onehot(p, f))
                if f == 0:
                    wait(act, s_g, p * 16)
                act.activation(emb_w[:, :, NG + f, :, :], xb[X[f]][:, 0:PAIR].rearrange("p (s q g) -> p s q g", s=2, q=4),
                               ACT.Copy).then_inc(s_xf[X[f]], 1)

            def copy_transposed(p, s, g):
                act.wait_ge(s_t, p * 2 * TG + s * TG + g + 1)
                act.activation(emb_w[:, s, FG * g:FG * g + FG, :, :],
                               tb[(s * TG + g) % 2][:, 0:FG * P].rearrange("p (f q b) -> p f q b", f=FG, q=4), ACT.Copy).then_inc(s_tf, 1)

            def copy_gram(p, s, k):
                act.wait_ge(s_g, p * 16 + s * NGB + k + 1)
                if k == 0:
                    wait(act, s_zt, (p - 1) * 2 + s + 1)
                for q in range(4):
                    end = min(FP * q + FP, GROWS)
                    ins = act.activation(
                        gram[s][FP * q:end, GB * k:GB * k + GB, :],
                        gb[0][FP * q:end, 0:GB * 4 * NF].rearrange("p (g c) -> p g c", g=GB)[:, :, NF * q:NF * q + NF],
                        ACT.Copy)
                ins.then_inc(s_gf[0], 1)

            def copy_inputs(p, s):
                act.wait_ge(s_x[1], x1_inputs(p, s))
                if s == 0:
                    wait(act, s_m, p * 4 - 2)
                act.activation(h0[:, :, s * P:s * P + P], xb[1][:, 0:KC * P].rearrange("p (c b) -> p c b", c=KC),
                               ACT.Copy).then_inc(s_xf[1], 1)

            def copy_layer(p, u):
                act.wait_ge(s_m, p * 4 + u + 1)
                if u < 2:
                    for c in range(2):
                        ins = act.activation(h1[:, 2 * u + c, :], mb[u][:, c * PAIR:c * PAIR + PAIR], ACT.Relu,
                                             bias=b1s[:, 2 * u + c:2 * u + c + 1])
                elif u == 2:
                    for c in range(2):
                        ins = act.activation(h2[:, c, :], mb[0][:, c * PAIR:c * PAIR + PAIR], ACT.Relu, bias=b2s[:, c:c + 1])
                else:
                    ins = act.activation(ysb[:, bass.ds(p * PAIR, PAIR)], mb[1][0:1, 0:PAIR], ACT.Copy)
                ins.then_inc(s_mf, 1)

            def copy_upper(f):
                act.wait_ge(s_up, f + 1)
                act.activation(tab[f][:, 0, :, :], upper_part(f), ACT.Copy).then_inc(s_upc, 1)

            def copy_tile_layer1(c, s):
                src = (mb[0], xb[0])[c // 2][:, c % 2 * P:c % 2 * P + P] if s == 0 else lb[c][:, 0:P]
                return act.activation(h1[:, c, s * P:s * P + P], src, ACT.Relu, bias=b1s[:, c:c + 1])

            def make_squares(f, half):
                if half == 0:
                    wait(act, s_oha, ACT_MADE.index(f))
                for t in range(KT[f] // 2):
                    row = tcol[KT[f]] + half * (KT[f] // 2) + t
                    ins = act.activation(squares[half][0:KR, t, :], idh[:, f, :], ACT.Square, bias=rown[:, row:row + 1], scale=-1.0)
                ins.then_inc(s_sq, 1)

            def cut_squares(f):
                if f >= RING:
                    act.wait_ge(s_x[X[f - RING]], x_onehot(0, f - RING))
                n = KT[f] // 2
                for half in range(2):
                    act.wait_ge(s_sq, 2 * ACT_MADE.index(f) + half + 1)
                    ins = act.activation(onehot[f % RING][:, half * n:half * n + n, :], squares[half][0:KR, 0:n, :], ACT.Relu,
                                         bias=one[:, 0:1], scale=-1.0)
                ins.then_inc(s_oha, 1)

            def step(p, first, last):
                copy_onehot(p, 0)
                if first:
                    copy_upper(2)
                    cut_squares(2)
                copy_transposed(p, 0, 0)
                copy_transposed(p, 0, 1)
                copy_onehot(p, 1)
                if first:
                    copy_upper(3)
                    make_squares(5, 0)
                copy_onehot(p, 2)
                if not first:
                    copy_inputs(p - 1, 1)
                copy_transposed(p, 0, 2)
                if first:
                    make_squares(5, 1)
                    copy_upper(4)
                copy_onehot(p, 3)
                if first:
                    cut_squares(5)
                else:
                    if not last:
                        cast_ids(p + 1)
                    copy_layer(p - 1, 0)
                    copy_layer(p - 1, 1)
                if first:
                    copy_upper(5)
                copy_onehot(p, 4)
                copy_transposed(p, 0, 3)
                if first:
                    copy_upper(6)
                copy_onehot(p, 5)
                copy_transposed(p, 0, 4)
                if first:
                    cast_ids(p + 1)
                copy_onehot(p, 6)
                for k in range(0, NGB, 2):
                    copy_gram(p, 0, k)
                    if k < NGB - 2:
                        copy_transposed(p, 1, k // 2)
                if not first:
                    copy_layer(p - 1, 2)
                copy_transposed(p, 1, 3)
                copy_transposed(p, 1, 4)
                if not first:
                    copy_layer(p - 1, 3)
                for k in range(0, NGB, 2):
                    copy_gram(p, 1, k)
                    if k == 2:
                        copy_inputs(p, 0)

            act.wait_ge(s_rowi, len(set(KT)))
            act.activation(rown[:, :], rown_i[:, :], ACT.Copy).then_inc(s_rown, 1)
            cast_ids(0, 0, EARLY)
            copy_upper(0)
            cast_ids(0, EARLY, NOH)
            act.wait_ge(s_rown, 1)
            act.wait_ge(s_idh, 2)
            act.wait_ge(s_zero, 4)
            make_squares(2, 0)
            make_squares(2, 1)
            copy_upper(1)
            step(0, True, False)
            with act.Fori(1, NPAIR - 1) as p:
                step(p, False, False)
            step(NPAIR - 1, False, True)
            for u in range(2):
                act.wait_ge(s_l, u + 1)
                copy_tile_layer1(2 * u, 0)
                ins = copy_tile_layer1(2 * u + 1, 0)
            ins.then_inc(s_la, 1)
            copy_inputs(NPAIR - 1, 1)
            act.wait_ge(s_l, 3)
            for c in range(H2 // P):
                ins = act.activation(h2[:, c, 0:P], mb[1][:, c * P:c * P + P], ACT.Relu, bias=b2s[:, c:c + 1])
            ins.then_inc(s_la, 1)
            for c in (0, 2):
                act.wait_ge(s_l, 4 + c)
                copy_tile_layer1(c, 1).then_inc(s_la, 1)
            act.wait_ge(s_l, 8)
            act.activation(h2[:, 0, P:PAIR], mb[0][:, 0:P], ACT.Relu, bias=b2s[:, 0:1]).then_inc(s_la, 1)
            act.wait_ge(s_l, 10)
            act.activation(ysb[:, BATCH - PAIR:BATCH], lb[0][0:1, 0:PAIR], ACT.Copy).then_inc(s_la, 1)

        @block.tensor
        def _(pe):
            def lookup(p, f, first=False):
                if first and f in ACT_MADE:
                    pe.wait_ge(s_oha, ACT_MADE.index(f) + 1)
                else:
                    pe.wait_ge(s_oh, made(p, f))
                if first:
                    pe.wait_ge(s_rest, f + 1)
                    pe.wait_ge(s_upc, f + 1)
                wait(pe, s_xf[X[f]], x_onehot(p, f) - 1)
                n = KT[f] * PARTS
                for i in range(n):
                    t, part = divmod(i, PARTS)
                    ins = pe.matmul(xb[X[f]][:, 0:PAIR], tab[f][:, part, t, :], onehot[f % RING][:, t, :],
                                    start=(i == 0), stop=(i == n - 1))
                ins.then_inc(s_x[X[f]], 1)

            def transpose_rows(p, s, g):
                pe.wait_ge(s_rows[s][g], (p + 1) * GATHERED)
                wait(pe, s_tf, p * 2 * TG + s * TG + g - 1)
                for j in range(FG):
                    ins = pe.transpose(tb[(s * TG + g) % 2][:, j * P:j * P + P], rows[s][:, FG * g + j, :], ident[:, :])
                ins.then_inc(s_t, 1)

            def gram_products(p, s, k):
                if k == 0:
                    pe.wait_ge(s_tf, p * 2 * TG + s * TG + TG)
                    pe.wait_ge(s_xf[X[NOH - 2]], x_onehot(p, NOH - 2))
                    pe.wait_ge(s_xf[X[NOH - 1]], x_onehot(p, NOH - 1))
                wait(pe, s_gf[k % 2], p * 8 + 4 * s + k // 2)
                for j in range(GB):
                    x = emb_g[:, s, GB * k + j, :, :]
                    ins = pe.matmul(gb[k % 2][0:GROWS, j * 4 * NF:(j + 1) * 4 * NF],
                                    x.rearrange("p q f -> p (q f)")[:, 0:GROWS], x[:, :, 0:NF],
                                    start=True, stop=True)
                ins.then_inc(s_g, 1)

            def transpose_inputs(p, s):
                pe.wait_ge(s_z, p * 2 + s + 1)
                pe.wait_ge(s_dense[s], p * 16 + 16)
                wait(pe, s_xf[1], x1_inputs(p, s) - 1)
                for c in range(KC):
                    ins = pe.transpose(xb[1][:, c * P:c * P + P], zin[s][:, c * P:c * P + P], ident[:, :])
                ins.then_inc(s_x[1], 1)

            def layer1(p, u):
                pe.wait_ge(s_xf[1], x1_inputs(p, 1))
                for c in (2 * u, 2 * u + 1):
                    for k in range(KC):
                        n = P if k < KC - 1 else LAST
                        ins = pe.matmul(mb[u][:, (c % 2) * PAIR:(c % 2 + 1) * PAIR], w1s[0:n, k, c * P:c * P + P],
                                        h0[0:n, k, :], start=(k == 0), stop=(k == KC - 1))
                ins.then_inc(s_m, 1)

            def layer2(p, c):
                if c == 0:
                    pe.wait_ge(s_mf, p * 4 + 2)
                for k in range(H1 // P):
                    ins = pe.matmul(mb[0][:, c * PAIR:(c + 1) * PAIR], w2s[:, k, c * P:c * P + P], h1[:, k, :],
                                    start=(k == 0), stop=(k == H1 // P - 1))
                if c == H2 // P - 1:
                    ins.then_inc(s_m, 1)

            def layer3(p):
                pe.wait_ge(s_mf, p * 4 + 3)
                for k in range(H2 // P):
                    ins = pe.matmul(mb[1][0:1, 0:PAIR], w3s[:, k:k + 1], h2[:, k, :], start=(k == 0), stop=(k == H2 // P - 1))
                ins.then_inc(s_m, 1)

            def tile_layer1(s):
                pe.wait_ge(s_xf[1], x1_inputs(NPAIR - 1, s))
                for c in range(H1 // P):
                    dst = (mb[0], xb[0])[c // 2][:, c % 2 * P:c % 2 * P + P] if s == 0 else lb[c][:, 0:P]
                    for k in range(KC):
                        n = P if k < KC - 1 else LAST
                        ins = pe.matmul(dst, w1s[0:n, k, c * P:c * P + P], h0[0:n, k, s * P:s * P + P],
                                        start=(k == 0), stop=(k == KC - 1))
                    if s == 1 or c % 2 == 1:
                        ins.then_inc(s_l, 1)

            def step(p, first, last):
                if first:
                    lookup(p, 0, first)
                transpose_rows(p, 0, 0)
                transpose_rows(p, 0, 1)
                lookup(p, 1, first)
                lookup(p, 2, first)
                if not first:
                    transpose_inputs(p - 1, 1)
                transpose_rows(p, 0, 2)
                lookup(p, 3, first)
                if not first:
                    layer1(p - 1, 0)
                    layer1(p - 1, 1)
                lookup(p, 4, first)
                transpose_rows(p, 0, 3)
                lookup(p, 5, first)
                transpose_rows(p, 0, 4)
                lookup(p, 6, first)
                if not first:
                    layer2(p - 1, 0)
                for k in range(NGB):
                    gram_products(p, 0, k)
                    if k in (1, 3, 5):
                        transpose_rows(p, 1, k // 2)
                if not first:
                    layer2(p - 1, 1)
                transpose_rows(p, 1, 3)
                if not last:
                    lookup(p + 1, 0)
                transpose_rows(p, 1, 4)
                if not first:
                    layer3(p - 1)
                for k in range(NGB):
                    gram_products(p, 1, k)
                    if k == 3:
                        transpose_inputs(p, 0)

            pe.wait_ge(s_ident, 2)
            pe.wait_ge(s_zero, 4)
            step(0, True, False)
            pe.wait_ge(s_wts, 16 * 6)
            with pe.Fori(1, NPAIR - 1) as p:
                step(p, False, False)
            q = NPAIR - 1
            step(q, False, True)
            tile_layer1(0)
            transpose_inputs(q, 1)
            pe.wait_ge(s_la, 1)
            pe.wait_ge(s_mf, 4 * q)
            for c in range(H2 // P):
                for k in range(H1 // P):
                    ins = pe.matmul(mb[1][:, c * P:c * P + P], w2s[:, k, c * P:c * P + P], h1[:, k, 0:P],
                                    start=(k == 0), stop=(k == H1 // P - 1))
            ins.then_inc(s_l, 1)
            tile_layer1(1)
            pe.wait_ge(s_la, 2)
            for k in range(H1 // P):
                pe.wait_ge((s_la, s_lv)[k % 2], (3, 1, 4, 2)[k])
                for c in range(H2 // P):
                    ins = pe.matmul(mb[c][:, 0:P], w2s[:, k, c * P:c * P + P], h1[:, k, P:PAIR],
                                    start=(k == 0), stop=(k == H1 // P - 1))
                    if k == H1 // P - 1:
                        ins.then_inc(s_l, 1)
            for s in range(2):
                if s == 1:
                    pe.wait_ge(s_la, 5)
                    pe.wait_ge(s_lv, 3)
                for k in range(H2 // P):
                    ins = pe.matmul(lb[0][0:1, s * P:s * P + P], w3s[:, k:k + 1], h2[:, k, s * P:s * P + P],
                                    start=(k == 0), stop=(k == H2 // P - 1))
            ins.then_inc(s_l, 1)


def kernel(**inputs):
    from concourse import bacc
    from concourse.bass_utils import run_bass_kernel_spmd

    ids = np.asarray(inputs["ids"])
    arrays = {"ids": ids, "ids_t": ids[:, ONEHOT].T, "dense": inputs["dense_ctx"],
              "w1": np.asarray(inputs["W_top1"])[first_layer_rows()], "b1": np.asarray(inputs["b_top1"]).reshape(-1, P).T,
              "w2": inputs["W_top2"], "b2": np.asarray(inputs["b_top2"]).reshape(-1, P).T,
              "w3": np.asarray(inputs["W_top3"]).reshape(-1, P).T}
    arrays.update({f"tbl_{f}": inputs[f"tbl_{f}"] for f in range(NF)})
    arrays = {k: np.ascontiguousarray(v) for k, v in arrays.items()}
    nc = bacc.Bacc("TRN2", target_bir_lowering=False, num_devices=1)
    ap = {k: nc.dram_tensor(k, v.shape, mybir.dt.from_np(v.dtype), kind="ExternalInput").ap() for k, v in arrays.items()}
    out = nc.dram_tensor("out", (BATCH, 1), mybir.dt.float32, kind="ExternalOutput").ap()
    dlrm_tower(nc, ap["ids"], ap["ids_t"], ap["dense"], [ap[f"tbl_{f}"] for f in range(NF)],
               ap["w1"], ap["b1"], ap["w2"], ap["b2"], ap["w3"], out)
    result = run_bass_kernel_spmd(nc, [arrays], core_ids=[0])
    return result.results[0]["out"]
```
